# Optimizing a Trainium2 kernel written in Bass

```python
import numpy as np
import jax
import jax.numpy as jnp

def _softmax(x, axis=-1):
    return jax.nn.softmax(x, axis=axis)

def _gelu(x):
    return jax.nn.gelu(x, approximate=True)

def _silu(x):
    return jax.nn.silu(x)

def _sigmoid(x):
    return jax.nn.sigmoid(x)

def _layernorm(x, axis=-1, eps=1e-05):
    m = jnp.mean(x, axis=axis, keepdims=True)
    v = jnp.var(x, axis=axis, keepdims=True)
    return (x - m) / jnp.sqrt(v + eps)

def _scatter_add(tgt, idx, src, axis=0):
    return tgt.at[idx].add(src)

def _segment_sum(src, seg, n):
    return jax.ops.segment_sum(src, seg, n)
kernel_name = 'mk_flamingo_gated_d2_seqx_r8_b23910'

def setup_inputs(seed: int=0):
    np.random.seed(seed)
    _w = jnp.asarray

    def _rec_inputs():
        import jax
        import jax.numpy as jnp
        _rk = jax.random.key(seed)
        x = -0.0002928 + 1 * jax.random.normal(jax.random.fold_in(_rk, 1), (8, 256, 128), jnp.float32)
        _lenS = 256 - jax.random.randint(jax.random.fold_in(_rk, 7), (8,), 0, max(1, 256 // 4) + 1, jnp.int32)
        _lenS2 = 256 - jax.random.randint(jax.random.fold_in(_rk, 8), (8,), 0, max(1, 256 // 4) + 1, jnp.int32)
        _ctx_1024P = jax.random.normal(jax.random.fold_in(_rk, 11), (8, 16, 128), jnp.float32)
        _ctx_1024c = jax.random.dirichlet(jax.random.fold_in(_rk, 511), 0.3 * jnp.ones((16,), jnp.float32), (8, 256))
        _ctx_1024t = jnp.einsum('bsk,bkd->bsd', _ctx_1024c, _ctx_1024P)
        _ctx_1024t = _ctx_1024t * jax.lax.rsqrt(jnp.mean(jnp.square(_ctx_1024t)) + 1e-12) * 0.953939
        ctx_1024 = -1.39393e-06 + 0.999914 * (_ctx_1024t + 0.3 * jax.random.normal(jax.random.fold_in(_rk, 611), (8, 256, 128), jnp.float32))
        _g = jax.random.normal(jax.random.fold_in(_rk, 9001), (2, 2), jnp.float32)
        _g = jnp.sign(_g) * jnp.maximum(jnp.abs(_g), 1.0) + (_g == 0) * 1.0
        g_xattn = _g[0]
        g_ffn = _g[1]
        return (x, ctx_1024, g_xattn, g_ffn)
    x, ctx_1024, g_xattn, g_ffn = _rec_inputs()

    def _L0_xattn_setup():
        import jax, jax.numpy as jnp
        import numpy as np
        EMBED_DIM = 128
        NUM_HEADS = 16
        HEAD_DIM = EMBED_DIM // NUM_HEADS
        key = jax.random.key(seed)
        ks = jax.random.split(key, 11)
        B, S, D = (2, 256, EMBED_DIM)
        scale = 1.0 / np.sqrt(D)
        inp = {'query': jax.random.normal(ks[0], (B, S, D), jnp.float32), 'key': jax.random.normal(ks[1], (B, S, D), jnp.float32), 'value': jax.random.normal(ks[2], (B, S, D), jnp.float32), 'Wq': jax.random.normal(ks[3], (D, D), jnp.float32) * scale, 'bq': jnp.zeros((D,), jnp.float32), 'Wk': jax.random.normal(ks[4], (D, D), jnp.float32) * scale, 'bk': jnp.zeros((D,), jnp.float32), 'Wv': jax.random.normal(ks[5], (D, D), jnp.float32) * scale, 'bv': jnp.zeros((D,), jnp.float32), 'Wo': jax.random.normal(ks[6], (D, D), jnp.float32) * scale, 'bo': jnp.zeros((D,), jnp.float32)}
        return inp
    _L0_xattn_all = _L0_xattn_setup()
    _L0_xattn_in = {k: v for k, v in _L0_xattn_all.items() if k in ('Wq', 'bq', 'Wk', 'bk', 'Wv', 'bv', 'Wo', 'bo')}
    del _L0_xattn_all

    def _L0_ffn_setup():
        import jax, jax.numpy as jnp
        import numpy as np
        B, N, D = (4, 512, 128)
        E, K, H, ITERS = (8, 2, 64, 2)
        DT = 0.1
        C = 2 * D

        def _gelu(x):
            return jax.nn.gelu(x, approximate=False)

        def _inl(ctrl, xs, vs, mu):
            a, b, g = jnp.split(ctrl, 3, axis=-1)
            v_next = jax.nn.sigmoid(a) * vs - jax.nn.softplus(b) * (xs - mu)
            x_next = xs + DT * jax.nn.sigmoid(g) * v_next
            return (x_next, v_next)

        def _experts(ctx, idx, w1, b1, w2, b2):
            out = jnp.zeros((ctx.shape[0], w2.shape[2]), ctx.dtype)
            for e in range(E):
                h = _gelu(ctx @ w1[e] + b1[e])
                o = h @ w2[e] + b2[e]
                out = out + jnp.where((idx == e)[:, None], o, jnp.float32(0))
            return out

        def _forward(x, integration_weight, mu, router_w1, router_b1, router_w2, router_b2, halt_w1, halt_b1, halt_w2, halt_b2, expert_w1, expert_b1, expert_w2, expert_b2, shared_w1, shared_b1, shared_w2, shared_b2, shared_weight, refine_w1, refine_b1, refine_w2, refine_b2):
            b, n, d = x.shape
            xf = x.reshape(b * n, d)
            logits = _gelu(xf @ router_w1 + router_b1) @ router_w2 + router_b2
            probs = jax.nn.softmax(logits, axis=-1)
            topk_p, topk_i = jax.lax.top_k(probs, K)
            topk_p = topk_p / jnp.sum(topk_p, axis=-1, keepdims=True)
            flat_idx = topk_i.reshape(-1)
            flat_w = topk_p.reshape(-1, 1)
            v = jnp.zeros_like(xf)
            integrated = xf
            for _ in range(ITERS):
                ctx = jnp.concatenate([integrated, v], axis=-1)
                shared_ctrl = _gelu(ctx @ shared_w1 + shared_b1) @ shared_w2 + shared_b2
                x_sh, v_sh = _inl(shared_ctrl, integrated, v, mu)
                sw = jax.nn.sigmoid(shared_weight)
                ctx_e = jnp.repeat(ctx, K, axis=0)
                x_e = jnp.repeat(integrated, K, axis=0)
                v_e = jnp.repeat(v, K, axis=0)
                ctrl = _experts(ctx_e, flat_idx, expert_w1, expert_b1, expert_w2, expert_b2)
                x_r, v_r = _inl(ctrl, x_e, v_e, mu)
                x_r = (x_r * flat_w).reshape(-1, K, d).sum(axis=1)
                v_r = (v_r * flat_w).reshape(-1, K, d).sum(axis=1)
                x_next = sw * x_sh + (1.0 - sw) * x_r
                v_next = sw * v_sh + (1.0 - sw) * v_r
                halt = jax.nn.sigmoid(_gelu(integrated @ halt_w1 + halt_b1) @ halt_w2 + halt_b2)
                integrated = integrated + halt * (x_next - integrated)
                v = v + halt * (v_next - v)
            refined = _gelu(integrated @ refine_w1 + refine_b1) @ refine_w2 + refine_b2
            out = xf + integration_weight * refined
            return out.reshape(b, n, d)
        key = jax.random.key(seed)
        ks = jax.random.split(key, 12)
        rn = lambda k, s, sc=0.02: jax.random.normal(k, s, dtype=jnp.float32) * sc
        z = lambda s: jnp.zeros(s, jnp.float32)
        return {'x': jax.random.normal(ks[0], (B, N, D), dtype=jnp.float32), 'integration_weight': jnp.full((D,), 0.5, jnp.float32), 'mu': z((D,)), 'router_w1': rn(ks[1], (D, D // 4)), 'router_b1': z((D // 4,)), 'router_w2': rn(ks[2], (D // 4, E)), 'router_b2': z((E,)), 'halt_w1': rn(ks[3], (D, D // 4)), 'halt_b1': z((D // 4,)), 'halt_w2': rn(ks[4], (D // 4, 1)), 'halt_b2': z((1,)), 'expert_w1': rn(ks[5], (E, C, H)), 'expert_b1': z((E, H)), 'expert_w2': rn(ks[6], (E, H, 3 * D)), 'expert_b2': z((E, 3 * D)), 'shared_w1': rn(ks[7], (C, H)), 'shared_b1': z((H,)), 'shared_w2': rn(ks[8], (H, 3 * D)), 'shared_b2': z((3 * D,)), 'shared_weight': jnp.float32(0.5), 'refine_w1': rn(ks[9], (D, 2 * D)), 'refine_b1': z((2 * D,)), 'refine_w2': rn(ks[10], (2 * D, D)), 'refine_b2': z((D,))}
    _L0_ffn_all = _L0_ffn_setup()
    _L0_ffn_in = {k: v for k, v in _L0_ffn_all.items() if k in ('integration_weight', 'mu', 'router_w1', 'router_b1', 'router_w2', 'router_b2', 'halt_w1', 'halt_b1', 'halt_w2', 'halt_b2', 'expert_w1', 'expert_b1', 'expert_w2', 'expert_b2', 'shared_w1', 'shared_b1', 'shared_w2', 'shared_b2', 'shared_weight', 'refine_w1', 'refine_b1', 'refine_w2', 'refine_b2')}
    del _L0_ffn_all

    def _L1_xattn_setup():
        import jax, jax.numpy as jnp
        import numpy as np
        key = jax.random.key(seed)
        k1, k2 = jax.random.split(key)
        hidden_states = jax.random.normal(k1, (8, 512, 128), dtype=jnp.float32)
        visual_hidden_state = jax.random.normal(k2, (8, 128, 128), dtype=jnp.float32)
        return {'hidden_states': hidden_states, 'visual_hidden_state': visual_hidden_state}
    _L1_xattn_all = _L1_xattn_setup()
    _L1_xattn_in = {k: v for k, v in _L1_xattn_all.items() if k in ()}
    del _L1_xattn_all

    def _L1_ffn_setup():
        import jax, jax.numpy as jnp
        import numpy as np
        E, D, DFF = (8, 128, 512)
        key = jax.random.key(seed)
        ks = jax.random.split(key, 10)
        s = 0.02
        return {'x': jax.random.normal(ks[0], (4, 256, D), dtype=jnp.float32), 'Wr': jax.random.normal(ks[1], (D, E), dtype=jnp.float32) * s, 'br': jnp.zeros((E,), dtype=jnp.float32), 'W1': jax.random.normal(ks[2], (E, D, DFF), dtype=jnp.float32) * s, 'b1': jnp.zeros((E, DFF), dtype=jnp.float32), 'W2': jax.random.normal(ks[3], (E, D, DFF), dtype=jnp.float32) * s, 'b2': jnp.zeros((E, DFF), dtype=jnp.float32), 'W3': jax.random.normal(ks[4], (E, DFF, D), dtype=jnp.float32) * s, 'b3': jnp.zeros((E, D), dtype=jnp.float32)}
    _L1_ffn_all = _L1_ffn_setup()
    _L1_ffn_in = {k: v for k, v in _L1_ffn_all.items() if k in ('Wr', 'br', 'W1', 'b1', 'W2', 'b2', 'W3', 'b3')}
    del _L1_ffn_all
    return {'x': x, 'ctx_1024': ctx_1024, 'g_xattn': g_xattn, 'g_ffn': g_ffn, 'L0_xattn_Wq': _L0_xattn_in['Wq'], 'L0_xattn_bq': _L0_xattn_in['bq'], 'L0_xattn_Wk': _L0_xattn_in['Wk'], 'L0_xattn_bk': _L0_xattn_in['bk'], 'L0_xattn_Wv': _L0_xattn_in['Wv'], 'L0_xattn_bv': _L0_xattn_in['bv'], 'L0_xattn_Wo': _L0_xattn_in['Wo'], 'L0_xattn_bo': _L0_xattn_in['bo'], 'L0_ffn_integration_weight': _L0_ffn_in['integration_weight'], 'L0_ffn_mu': _L0_ffn_in['mu'], 'L0_ffn_router_w1': _L0_ffn_in['router_w1'], 'L0_ffn_router_b1': _L0_ffn_in['router_b1'], 'L0_ffn_router_w2': _L0_ffn_in['router_w2'], 'L0_ffn_router_b2': _L0_ffn_in['router_b2'], 'L0_ffn_halt_w1': _L0_ffn_in['halt_w1'], 'L0_ffn_halt_b1': _L0_ffn_in['halt_b1'], 'L0_ffn_halt_w2': _L0_ffn_in['halt_w2'], 'L0_ffn_halt_b2': _L0_ffn_in['halt_b2'], 'L0_ffn_expert_w1': _L0_ffn_in['expert_w1'], 'L0_ffn_expert_b1': _L0_ffn_in['expert_b1'], 'L0_ffn_expert_w2': _L0_ffn_in['expert_w2'], 'L0_ffn_expert_b2': _L0_ffn_in['expert_b2'], 'L0_ffn_shared_w1': _L0_ffn_in['shared_w1'], 'L0_ffn_shared_b1': _L0_ffn_in['shared_b1'], 'L0_ffn_shared_w2': _L0_ffn_in['shared_w2'], 'L0_ffn_shared_b2': _L0_ffn_in['shared_b2'], 'L0_ffn_shared_weight': _L0_ffn_in['shared_weight'], 'L0_ffn_refine_w1': _L0_ffn_in['refine_w1'], 'L0_ffn_refine_b1': _L0_ffn_in['refine_b1'], 'L0_ffn_refine_w2': _L0_ffn_in['refine_w2'], 'L0_ffn_refine_b2': _L0_ffn_in['refine_b2'], 'L1_ffn_Wr': _L1_ffn_in['Wr'], 'L1_ffn_br': _L1_ffn_in['br'], 'L1_ffn_W1': _L1_ffn_in['W1'], 'L1_ffn_b1': _L1_ffn_in['b1'], 'L1_ffn_W2': _L1_ffn_in['W2'], 'L1_ffn_b2': _L1_ffn_in['b2'], 'L1_ffn_W3': _L1_ffn_in['W3'], 'L1_ffn_b3': _L1_ffn_in['b3']}

def reference(x, ctx_1024, g_xattn, g_ffn, L0_xattn_Wq, L0_xattn_bq, L0_xattn_Wk, L0_xattn_bk, L0_xattn_Wv, L0_xattn_bv, L0_xattn_Wo, L0_xattn_bo, L0_ffn_integration_weight, L0_ffn_mu, L0_ffn_router_w1, L0_ffn_router_b1, L0_ffn_router_w2, L0_ffn_router_b2, L0_ffn_halt_w1, L0_ffn_halt_b1, L0_ffn_halt_w2, L0_ffn_halt_b2, L0_ffn_expert_w1, L0_ffn_expert_b1, L0_ffn_expert_w2, L0_ffn_expert_b2, L0_ffn_shared_w1, L0_ffn_shared_b1, L0_ffn_shared_w2, L0_ffn_shared_b2, L0_ffn_shared_weight, L0_ffn_refine_w1, L0_ffn_refine_b1, L0_ffn_refine_w2, L0_ffn_refine_b2, L1_ffn_Wr, L1_ffn_br, L1_ffn_W1, L1_ffn_b1, L1_ffn_W2, L1_ffn_b2, L1_ffn_W3, L1_ffn_b3):
    import jax
    import jax.numpy as jnp

    def _L0_xattn_ref(query, key, value, Wq, bq, Wk, bk, Wv, bv, Wo, bo):
        import jax, jax.numpy as jnp
        import numpy as np
        EMBED_DIM = 128
        NUM_HEADS = 16
        HEAD_DIM = EMBED_DIM // NUM_HEADS
        B, S, D = query.shape
        H, Hd = (NUM_HEADS, HEAD_DIM)

        def split_heads(x):
            return x.reshape(B, S, H, Hd).transpose(0, 2, 1, 3)
        Q = split_heads(query @ Wq.T + bq)
        K = split_heads(key @ Wk.T + bk)
        V = split_heads(value @ Wv.T + bv)
        scores = jnp.einsum('bhqd,bhkd->bhqk', Q, K) / np.sqrt(Hd).astype(jnp.float32)
        attn = jax.nn.softmax(scores, axis=-1)
        out = jnp.einsum('bhqk,bhkd->bhqd', attn, V)
        out = out.transpose(0, 2, 1, 3).reshape(B, S, D)
        return out @ Wo.T + bo

    def _L0_ffn_ref(x, integration_weight, mu, router_w1, router_b1, router_w2, router_b2, halt_w1, halt_b1, halt_w2, halt_b2, expert_w1, expert_b1, expert_w2, expert_b2, shared_w1, shared_b1, shared_w2, shared_b2, shared_weight, refine_w1, refine_b1, refine_w2, refine_b2):
        import jax, jax.numpy as jnp
        import numpy as np
        B, N, D = (4, 512, 128)
        E, K, H, ITERS = (8, 2, 64, 2)
        DT = 0.1
        C = 2 * D

        def _gelu(x):
            return jax.nn.gelu(x, approximate=False)

        def _inl(ctrl, xs, vs, mu):
            a, b, g = jnp.split(ctrl, 3, axis=-1)
            v_next = jax.nn.sigmoid(a) * vs - jax.nn.softplus(b) * (xs - mu)
            x_next = xs + DT * jax.nn.sigmoid(g) * v_next
            return (x_next, v_next)

        def _experts(ctx, idx, w1, b1, w2, b2):
            out = jnp.zeros((ctx.shape[0], w2.shape[2]), ctx.dtype)
            for e in range(E):
                h = _gelu(ctx @ w1[e] + b1[e])
                o = h @ w2[e] + b2[e]
                out = out + jnp.where((idx == e)[:, None], o, jnp.float32(0))
            return out

        def _forward(x, integration_weight, mu, router_w1, router_b1, router_w2, router_b2, halt_w1, halt_b1, halt_w2, halt_b2, expert_w1, expert_b1, expert_w2, expert_b2, shared_w1, shared_b1, shared_w2, shared_b2, shared_weight, refine_w1, refine_b1, refine_w2, refine_b2):
            b, n, d = x.shape
            xf = x.reshape(b * n, d)
            logits = _gelu(xf @ router_w1 + router_b1) @ router_w2 + router_b2
            probs = jax.nn.softmax(logits, axis=-1)
            topk_p, topk_i = jax.lax.top_k(probs, K)
            topk_p = topk_p / jnp.sum(topk_p, axis=-1, keepdims=True)
            flat_idx = topk_i.reshape(-1)
            flat_w = topk_p.reshape(-1, 1)
            v = jnp.zeros_like(xf)
            integrated = xf
            for _ in range(ITERS):
                ctx = jnp.concatenate([integrated, v], axis=-1)
                shared_ctrl = _gelu(ctx @ shared_w1 + shared_b1) @ shared_w2 + shared_b2
                x_sh, v_sh = _inl(shared_ctrl, integrated, v, mu)
                sw = jax.nn.sigmoid(shared_weight)
                ctx_e = jnp.repeat(ctx, K, axis=0)
                x_e = jnp.repeat(integrated, K, axis=0)
                v_e = jnp.repeat(v, K, axis=0)
                ctrl = _experts(ctx_e, flat_idx, expert_w1, expert_b1, expert_w2, expert_b2)
                x_r, v_r = _inl(ctrl, x_e, v_e, mu)
                x_r = (x_r * flat_w).reshape(-1, K, d).sum(axis=1)
                v_r = (v_r * flat_w).reshape(-1, K, d).sum(axis=1)
                x_next = sw * x_sh + (1.0 - sw) * x_r
                v_next = sw * v_sh + (1.0 - sw) * v_r
                halt = jax.nn.sigmoid(_gelu(integrated @ halt_w1 + halt_b1) @ halt_w2 + halt_b2)
                integrated = integrated + halt * (x_next - integrated)
                v = v + halt * (v_next - v)
            refined = _gelu(integrated @ refine_w1 + refine_b1) @ refine_w2 + refine_b2
            out = xf + integration_weight * refined
            return out.reshape(b, n, d)
        return _forward(x, integration_weight, mu, router_w1, router_b1, router_w2, router_b2, halt_w1, halt_b1, halt_w2, halt_b2, expert_w1, expert_b1, expert_w2, expert_b2, shared_w1, shared_b1, shared_w2, shared_b2, shared_weight, refine_w1, refine_b1, refine_w2, refine_b2)

    def _L1_xattn_ref(hidden_states, visual_hidden_state):
        import jax, jax.numpy as jnp
        import numpy as np
        fusion_scores = jnp.einsum('bsd,bvd->bsv', hidden_states, visual_hidden_state)
        fusion_probs = jax.nn.softmax(fusion_scores, axis=-1)
        fusion_output = jnp.einsum('bsv,bvd->bsd', fusion_probs, visual_hidden_state)
        return fusion_output

    def _L1_ffn_ref(x, Wr, br, W1, b1, W2, b2, W3, b3):
        import jax, jax.numpy as jnp
        import numpy as np
        E, D, DFF = (8, 128, 512)
        b, s, d = x.shape
        xt = x.reshape(b * s, d)
        logits = xt @ Wr + br
        pr, idx = jax.lax.top_k(logits, 2)
        w = jax.nn.softmax(pr, axis=-1)
        onehot = jax.nn.one_hot(idx, W1.shape[0], dtype=x.dtype)
        cw = jnp.einsum('tk,tke->te', w, onehot)
        y = jnp.zeros_like(xt)
        for e in range(W1.shape[0]):
            h = jax.nn.silu(xt @ W1[e] + b1[e]) * (xt @ W2[e] + b2[e])
            y = y + (h @ W3[e] + b3[e]) * cw[:, e:e + 1]
        return y.reshape(b, s, d)
    x = x + jnp.tanh(g_xattn[0]) * _L0_xattn_ref(_layernorm(x, axis=-1), ctx_1024, ctx_1024, L0_xattn_Wq, L0_xattn_bq, L0_xattn_Wk, L0_xattn_bk, L0_xattn_Wv, L0_xattn_bv, L0_xattn_Wo, L0_xattn_bo)
    x = x + jnp.tanh(g_ffn[0]) * _L0_ffn_ref(_layernorm(x, axis=-1), L0_ffn_integration_weight, L0_ffn_mu, L0_ffn_router_w1, L0_ffn_router_b1, L0_ffn_router_w2, L0_ffn_router_b2, L0_ffn_halt_w1, L0_ffn_halt_b1, L0_ffn_halt_w2, L0_ffn_halt_b2, L0_ffn_expert_w1, L0_ffn_expert_b1, L0_ffn_expert_w2, L0_ffn_expert_b2, L0_ffn_shared_w1, L0_ffn_shared_b1, L0_ffn_shared_w2, L0_ffn_shared_b2, L0_ffn_shared_weight, L0_ffn_refine_w1, L0_ffn_refine_b1, L0_ffn_refine_w2, L0_ffn_refine_b2)
    x = x + jnp.tanh(g_xattn[1]) * _L1_xattn_ref(_layernorm(x, axis=-1), ctx_1024)
    x = x + jnp.tanh(g_ffn[1]) * _L1_ffn_ref(_layernorm(x, axis=-1), L1_ffn_Wr, L1_ffn_br, L1_ffn_W1, L1_ffn_b1, L1_ffn_W2, L1_ffn_b2, L1_ffn_W3, L1_ffn_b3)
    return x

_drawn_inputs = setup_inputs


def setup_inputs(seed=0):
    import zlib

    import numpy as np

    out = dict(_drawn_inputs(seed))
    spreads = {'g_ffn': (-1.0, 0.6),
     'L0_xattn_bq': (0.0, 0.1),
     'L0_xattn_bk': (0.0, 2.0),
     'L0_xattn_bv': (0.0, 0.1),
     'L0_xattn_bo': (0.0, 0.1),
     'L0_ffn_integration_weight': (0.5, 0.2),
     'L0_ffn_mu': (0.0, 0.8),
     'L0_ffn_router_b1': (0.0, 2.0),
     'L0_ffn_router_b2': (0.0, 2.0),
     'L0_ffn_halt_b1': (0.0, 0.8),
     'L0_ffn_expert_b1': (0.0, 2.0),
     'L0_ffn_expert_b2': (0.0, 0.8),
     'L0_ffn_shared_b1': (0.0, 0.8),
     'L0_ffn_shared_b2': (0.0, 0.8),
     'L0_ffn_refine_b1': (0.0, 0.1),
     'L0_ffn_refine_b2': (0.0, 0.1),
     'L1_ffn_br': (0.0, 0.1),
     'L1_ffn_b1': (0.0, 0.8),
     'L1_ffn_b2': (0.0, 0.8),
     'L1_ffn_b3': (0.0, 0.698)}
    factors = {'L0_ffn_router_w1': 32.105,
     'L0_ffn_router_w2': 8.0,
     'L0_ffn_halt_w1': 8.0,
     'L0_ffn_halt_w2': 8.0,
     'L0_ffn_expert_w1': 8.0,
     'L0_ffn_expert_w2': 8.0,
     'L0_ffn_shared_w1': 8.0,
     'L0_ffn_shared_w2': 8.0,
     'L1_ffn_W1': 7.949,
     'L1_ffn_W2': 7.955,
     'L1_ffn_W3': 7.297}
    for name, (base, spread) in spreads.items():
        noise = np.random.default_rng([zlib.crc32(name.encode()), seed]).standard_normal(out[name].shape)
        drawn = base * np.exp(spread * noise) if base else spread * noise
        out[name] = jnp.asarray(drawn.astype(out[name].dtype))
    for name, factor in factors.items():
        out[name] = (out[name] * factor).astype(out[name].dtype)
    return out
```

```python
from contextlib import ExitStack

import concourse.bass as bass
from concourse import mybir

F32 = mybir.dt.float32
F32R = mybir.dt.float32r
BF16 = mybir.dt.bfloat16
U32 = mybir.dt.uint32
U16 = mybir.dt.uint16
F8 = mybir.dt.float8e4
ALU = mybir.AluOpType
ACT = mybir.ActivationFunctionType
AX = mybir.AxisListType

B, S, D = 8, 256, 128
T = B * S
P = 128
NT = T // P
CH = 512
NC = T // CH
TC = CH // P
BC = CH // S
H, HD = 16, 8
PAIRS = H // 2
GROUPS = H // 4
NEXT_PAIR_AFTER = (2, 4, 6, 7, 8, 9, 11, 12)
ROWS = 6 * HD
EPS = 1e-5
E = 8
HID = 64
DT = 0.1
FF = 512
MT = FF // P
ONE_BF16 = 0x3F80
CAP = 40.0


class Chain:

    def __init__(self, engine, semaphore):
        self.engine, self.semaphore, self.n = engine, semaphore, 0

    def then(self, instruction):
        instruction.then_inc(self.semaphore, 1)
        self.n += 1

    def wait(self):
        self.engine.wait_ge(self.semaphore, self.n)


def flamingo(nc, a, out):
    ctx = ExitStack()
    with ctx:
        def sb(name, shape, dt=F32):
            return ctx.enter_context(nc.sbuf_tensor(name, shape, dt))

        def sem(name):
            return ctx.enter_context(nc.semaphore(name))

        x = sb("x", [P, NT, D])
        xn = sb("xn", [P, NT, D])
        xT = sb("xT", [P, T])
        ident = sb("ident", [P, P])
        identb = sb("identb", [P, P], BF16)
        stats = sb("stats", [P, NT, 6])
        meanvar = sb("meanvar", [P, NT, 2])
        rstd = sb("rstd", [P, NT])
        minus_half = sb("minus_half", [P, NT])
        gates = sb("gates", [P, 4])
        tg = sb("tg", [P, 4])
        rw1 = sb("rw1", [P, 32])
        rw2 = sb("rw2", [32, E])
        rb1 = sb("rb1", [32, 1])
        rb2 = sb("rb2", [P, E])
        ew1 = sb("ew1", [P, 2, E * HID])
        eb1 = sb("eb1", [P, 4])
        ew2 = sb("ew2", [P, 4, 3 * D])
        eb2 = sb("eb2", [P, 3 * D])
        choice_rows = sb("choice_rows", [P, 6])
        eb2_parts = sb("eb2_parts", [P, 2, 3 * D], BF16)
        eb2_rows = sb("eb2_rows", [P, 2, 3 * D], BF16)
        sw1 = sb("sw1", [P, 2, 96])
        sb1 = sb("sb1", [96, 1])
        sw2 = sb("sw2", [96, 3 * D])
        sb2 = sb("sb2", [P, 3])
        hw2 = sb("hw2", [96, P])
        hb2 = sb("hb2", [P, 1])
        mu = sb("mu", [P, 1])
        shared_w = sb("shared_w", [P, 4])
        iota24 = sb("iota24", [P, 24])
        fw1 = sb("fw1", [P, 2 * D])
        fb1 = sb("fb1", [P, 2])
        fw2 = sb("fw2", [P, 2, D])
        iw = sb("iw", [P, D])
        fb2 = sb("fb2", [P, D])
        stage_a = ctx.enter_context(ExitStack())

        def sa(name, shape, dt=F32):
            return stage_a.enter_context(nc.sbuf_tensor(name, shape, dt))

        ctxT = sa("ctxT", [P, T])
        wqT = sa("wqT", [P, D])
        wkT = sa("wkT", [P, D])
        wvT = sa("wvT", [P, D])
        wo = sa("wo", [P, GROUPS, D])
        qk_bias = sa("qk_bias", [P, 2])
        bv = sa("bv", [P, D])
        bo = sa("bo", [P, D])
        qk = sa("qk", [P, 2, CH])
        rest = sa("rest", [P, 2, CH])
        parts = sa("parts", [P, 2, 3, CH], BF16)
        qs = sa("qs", [P, PAIRS, T], BF16)
        ks = sa("ks", [P, PAIRS, 2, T], BF16)
        v_all = xT[:].rearrange("p (t h d) -> p t h d", h=H, d=HD)
        v_aug = sa("v_aug", [P, BC, 2, H, 32])
        probs = sa("probs", [P, 2, 4, 2, S])
        negmax = sa("negmax", [P, PAIRS, 2, 2])
        max_rest = sa("max_rest", [P, PAIRS, 2, 2])
        max_parts = sa("max_parts", [P, 2, PAIRS, 2, 3], BF16)
        sumsT = sa("sumsT", [P, CH // 32, 32])
        recip = sa("recip", [P, CH // 32])
        recips = sa("recips", [P, 2, S])
        attnT = sa("attnT", [P, BC, GROUPS, S])

        def parts_view(memory):
            return memory[:, 0:3 * CH].bitcast(BF16).rearrange("p (s r n) -> p s r n", s=2, r=3)

        parts_of = [parts[:], parts_view(attnT[:].rearrange("p b g q -> p (b g q)")),
                    parts_view(probs[:, 1].rearrange("p h k q -> p (h k q)")), parts[:]]
        stage_a.close()

        stage_b = ExitStack()

        def sm(name, shape, dt=F32):
            return stage_b.enter_context(nc.sbuf_tensor(name, shape, dt))

        hidden = sm("hidden", [P, 2, 4, NC, CH])
        hidden_end = nc.sbuf_base
        chosen = sm("chosen", [P, 2, 4, NC, CH], F8)
        shared_h = sm("shared_h", [96, NC, CH])
        soft = sm("soft", [P, 3, 2, CH])
        v = sm("v", [P, NC, CH])
        weight = sm("weight", [P, 2, NC, CH])
        sig_g = sm("sig_g", [P, 3, CH])
        sig_a = sm("sig_a", [P, 3, CH])
        halt = sm("halt", [P, CH])
        unmasked = sm("unmasked", [P, 2, CH])
        routeT = sm("routeT", [P, NC, CH], BF16)
        w1t = sm("w1t", [P, 3, CH])
        w2t = sm("w2t", [P, 2, CH])
        hf = hidden[:].rearrange("p k j c n -> p (k j c n)")
        route = hf[:, 0:2048].rearrange("p (t n) -> p t n", n=P)
        routeT32 = hf[:, 2048:4096].rearrange("p (c n) -> p c n", n=CH)
        router_h = hf[0:32, 4096:6144].rearrange("p (c n) -> p c n", n=CH)
        logits = hf[:, 6144:6272].rearrange("p (t n) -> p t n", n=E)
        top = hf[:, 6272:6400].rearrange("p (t n) -> p t n", n=E)
        top_at = hf[:, 6400:6528].rearrange("p (t n) -> p t n", n=E).bitcast(U32)
        top_atf = hf[:, 6528:6560].rearrange("p (t n) -> p t n", n=2)
        gap = hf[:, 6560:6576]
        w_first = hf[:, 6576:6592]
        choice_sel = hf[:, 6656:6656 + 512].bitcast(BF16).rearrange("p (k j n) -> p k j n", k=2, j=4)
        weight_sel = hf[:, 7168:7168 + 256].rearrange("p (k n) -> p k n", k=2)
        stage_b.close()

        stage_c = ExitStack()

        def sc(name, shape, dt=F32):
            return stage_c.enter_context(nc.sbuf_tensor(name, shape, dt))

        ctxT2 = sc("ctxT2", [P, T])
        ctxm = sc("ctxm", [P, NT, D])
        w12 = sc("w12", [P, 2, 2, FF])
        w3 = sc("w3", [P, 2, MT, D])
        b12 = sc("b12", [P, 2, E, MT])
        b3 = sc("b3", [E, D])
        wr = sc("wr", [P, E])
        br = sc("br", [P, E])
        iota8 = sc("iota8", [P, E])
        assert nc.sbuf_base <= hidden_end
        probs2 = sc("probs2", [P, 2, 2, S])
        probsT = sc("probsT", [P, 2, 2, S])
        negmax2 = sc("negmax2", [P, B, 2])
        sums2 = sc("sums2", [P, B, 2])
        w12_hi = sc("w12_hi", [P, 2, 2, FF], F32R)
        w12_lo = sc("w12_lo", [P, 2, 2, FF], F32R)
        xT_hi = sc("xT_hi", [P, T], F32R)
        xT_lo = sc("xT_lo", [P, T], F32R)
        silu_g = sc("silu_g", [P, 2, CH])
        gated = sc("gated", [P, 2, MT, CH])
        logits2 = sc("logits2", [P, NT, E])
        top2 = sc("top2", [P, NT, E])
        top2_at = sc("top2_at", [P, NT, E], U32)
        top2_atf = sc("top2_atf", [P, NT, 2])
        is_top = sc("is_top", [P, 2, NT, E])
        gap2 = sc("gap2", [P, NT])
        w_top = sc("w_top", [P, 2, NT])
        share = sc("share", [P, NT, E])
        shareT = sc("shareT", [E, NC, CH])
        stage_c.close()

        stacked = nc.dram_tensor("stacked", [2, D, 6, T], BF16).ap()

        bank = [ctx.enter_context(nc.psum_tensor(f"bank{i}", [P, CH], F32)) for i in range(8)]
        s1 = [(0, 1), (2, 3)]
        s2 = [bank[4], bank[5]]
        o = [bank[6], bank[7]]

        consts_in = sem("consts_in")
        x_in = [sem(f"x_in{c}") for c in range(NC)]
        ctx_in = sem("ctx_in")
        stats_ready = sem("stats_ready")
        rstd_ready = sem("rstd_ready")
        tg_ready = sem("tg_ready")
        bo_gated = sem("bo_gated")
        xb_ready = sem("xb_ready")
        xn_ready = sem("xn_ready")
        xT_psum = sem("xT_psum")
        xT_ready = sem("xT_ready")
        qkv_psum = sem("qkv_psum")
        qk_high = sem("qk_high")
        qk_used = sem("qk_used")
        v_ready = sem("v_ready")
        parts_ready = sem("parts_ready")
        stacked_out = [sem(f"stacked_out{c}") for c in range(NC)]
        stacks_in = [sem(f"stacks_in{c}") for c in range(NC)]
        ks_zero = sem("ks_zero")
        v_aug_ready = sem("v_aug_ready")
        s1_ready = sem("s1_ready")
        max_done = sem("max_done")
        max_parts_ready = sem("max_parts_ready")
        maxT_psum = sem("maxT_psum")
        maxT_ready = sem("maxT_ready")
        s2_ready = sem("s2_ready")
        exp_done = sem("exp_done")
        pv_done = sem("pv_done")
        attn_ready = sem("attn_ready")
        y_psum = sem("y_psum")
        x1_ready = sem("x1_ready")
        dve_step = sem("dve_step")
        pool_step = sem("pool_step")
        out_done = sem("out_done")

        weights_in = sem("weights_in")
        route_zero = sem("route_zero")
        eb2_ready = sem("eb2_ready")
        selectors_in = sem("selectors_in")
        router_psum = sem("router_psum")
        router_h_ready = sem("router_h_ready")
        logits_psum = sem("logits_psum")
        gap_ready = sem("gap_ready")
        exp_gap_ready = sem("exp_gap_ready")
        route_ready = sem("route_ready")
        routeT_psum = sem("routeT_psum")
        routeT_ready = sem("routeT_ready")
        routeT32_ready = sem("routeT32_ready")
        chosen_psum = sem("chosen_psum")
        chosen_ready = sem("chosen_ready")
        weight_psum = sem("weight_psum")
        weight_ready = sem("weight_ready")
        hidden_psum = sem("hidden_psum")
        gelu_done = sem("gelu_done")
        masked_first = sem("masked_first")
        masked_second = sem("masked_second")
        soft_psum = sem("soft_psum")
        capped_ready = sem("capped_ready")
        ln_done = sem("ln_done")
        soft_done = sem("soft_done")
        gate_psum = sem("gate_psum")
        sigmoid_done = sem("sigmoid_done")
        state_ready = sem("state_ready")
        refine_psum = sem("refine_psum")
        refine_h_ready = sem("refine_h_ready")
        refined_psum = sem("refined_psum")
        x2_ready = sem("x2_ready")
        act_step = sem("act_step")
        ctx2_in = sem("ctx2_in")
        small2_in = sem("small2_in")
        w12_ready = sem("w12_ready")
        xT_hi_ready = sem("xT_hi_ready")
        xT_lo_ready = sem("xT_lo_ready")
        w_in = [sem(f"w_in{e}") for e in range(E)]
        scores_psum = sem("scores_psum")
        negmax2_ready = sem("negmax2_ready")
        exp2_done = sem("exp2_done")
        probsT_psum = sem("probsT_psum")
        probsT_ready = sem("probsT_ready")
        fused_psum = sem("fused_psum")
        x3_ready = sem("x3_ready")
        logits2_psum = sem("logits2_psum")
        gap2_ready = sem("gap2_ready")
        w2nd_ready = sem("w2nd_ready")
        share_ready = sem("share_ready")
        shareT_psum = sem("shareT_psum")
        shareT_ready = sem("shareT_ready")
        bias3_psum = sem("bias3_psum")
        bias3_added = sem("bias3_added")
        up_psum = sem("up_psum")
        silu_done = sem("silu_done")
        gated_ready = sem("gated_ready")
        down_psum = sem("down_psum")
        added = sem("added")
        fb2_ready = sem("fb2_ready")

        N_CONSTS = 9
        N_WEIGHTS = 23
        block = ctx.enter_context(nc.Block())

        def chunk(c):
            return slice(c * CH, (c + 1) * CH)

        def gate_use(it, c):
            return (4 + 3 * it) * c + 4 * NC * it

        @block.sync
        def _(sp):
            xv = a["x"].rearrange("(t p) f -> p t f", p=P)
            sp.dma_start(x[:, 0:TC, :], xv[:, 0:TC, :]).then_inc(x_in[0], 16)
            for dst, src in ((ident, a["ident"]), (wqT, a["wqT"]), (wkT, a["wkT"]), (wvT, a["wvT"])):
                sp.dma_start(dst[:], src).then_inc(consts_in, 16)
            sp.dma_start(ctxT[:], a["ctxT"]).then_inc(ctx_in, 16)
            for c in range(1, NC):
                sp.dma_start(x[:, c * TC:(c + 1) * TC, :], xv[:, c * TC:(c + 1) * TC, :]).then_inc(x_in[c], 16)

            for dst, src in ((rw1, "rw1"), (rw2, "rw2"), (rb1, "rb1"), (ew1, "ew1"), (eb1, "eb1"), (ew2, "ew2"), (eb2, "eb2"),
                             (choice_rows, "choice_rows"), (sw1, "sw1"), (sb1, "sb1"), (sw2, "sw2"), (sb2, "sb2"), (hw2, "hw2"),
                             (mu, "mu"), (iota24, "iota24"), (fw1, "fw1"), (fb1, "fb1"), (fw2, "fw2")):
                sp.dma_start(dst[:], a[src]).then_inc(weights_in, 16)
            for dst, src in ((rb2, "rb2"), (hb2, "hb2"), (iw, "iw"), (fb2, "fb2")):
                sp.dma_start(dst[:], a[src].partition_broadcast(P)).then_inc(weights_in, 16)
            sp.dma_start(shared_w[:, 0:1], a["shared_w"].partition_broadcast(P)).then_inc(weights_in, 16)

            for c in range(NC):
                sp.wait_ge(parts_ready, c + 1)
                pc = parts_of[c]
                for s, r0, r1, lo in ((0, 0, 3, 0), (0, 3, 4, 2), (0, 4, 6, 1)):
                    sp.dma_start(stacked[s, :, r0:r1, chunk(c)], pc[:, s, lo:lo + r1 - r0, :]).then_inc(stacked_out[c], 16)
                for r0, r1, part in ((0, 3, 2), (3, 5, 1), (5, 6, 0)):
                    sp.dma_start(stacked[1, :, r0:r1, chunk(c)],
                                 pc[:, 1, part:part + 1, :].to_broadcast([P, r1 - r0, CH])).then_inc(stacked_out[c], 16)
                sp.wait_ge(stacked_out[c], 96)
                sp.wait_ge(ks_zero, c + 1)
                for h in range(2):
                    rows = slice(ROWS * h, ROWS * h + ROWS)
                    view = stacked.rearrange("s (p a d) r n -> s a (d r) p n", a=2, d=HD)
                    sp.dma_start(qs[rows, :, chunk(c)], view[0, h, :, :, chunk(c)]).then_inc(stacks_in[c], 16)
                    sp.dma_start(ks[rows, :, h, chunk(c)], view[1, h, :, :, chunk(c)]).then_inc(stacks_in[c], 16)
                    sp.dma_start(ks[96:102, :, h, chunk(c)].bitcast(U16), a["max_rows"][h].rearrange("r (p n) -> r p n", p=PAIRS)).then_inc(stacks_in[c], 16)

            sp.wait_ge(x1_ready, B)
            sp.dma_start(choice_sel.bitcast(U16), a["choice_sel"]).then_inc(selectors_in, 16)
            sp.dma_start(weight_sel, a["weight_sel"]).then_inc(selectors_in, 16)

            sp.wait_ge(gate_psum, gate_use(1, NC))
            sp.dma_start(ctxT2[:], a["ctxT"]).then_inc(ctx2_in, 16)
            cv = a["ctx"].rearrange("(t p) f -> p t f", p=P)
            for c in range(NC):
                sp.dma_start(ctxm[:, c * TC:(c + 1) * TC, :], cv[:, c * TC:(c + 1) * TC, :]).then_inc(ctx2_in, 16)
            for dst, src in ((wr, a["wr"]), (br, a["br"].partition_broadcast(P)), (b12, a["b12"]), (b3, a["b3"]), (iota8, a["iota8"])):
                sp.dma_start(dst[:], src).then_inc(small2_in, 16)
            for e in range(E):
                if e >= 2:
                    sp.wait_ge(down_psum, NC * (e - 1))
                    sp.wait_ge(w12_ready, e - 1)
                sp.dma_start(w12[:, e % 2, 0, :], a["w1"][e]).then_inc(w_in[e], 16)
                sp.dma_start(w12[:, e % 2, 1, :], a["w2"][e]).then_inc(w_in[e], 16)
                sp.dma_start(w3[:, e % 2, :, :], a["w3"][e]).then_inc(w_in[e], 16)

            ov = out.rearrange("(t p) f -> p t f", p=P)
            for c in range(NC):
                sp.wait_ge(added, NC * (E - 1) + c + 1)
                sp.dma_start(ov[:, c * TC:(c + 1) * TC, :], x[:, c * TC:(c + 1) * TC, :]).then_inc(out_done, 16)
            sp.wait_ge(out_done, 16 * NC)

        @block.gpsimd
        def _(pool):
            steps = Chain(pool, pool_step)
            steps.then(nc.gpsimd.memset(minus_half[:], -0.5))

            def rstd_of_chunk(norm, c):
                pool.wait_ge(stats_ready, NC * norm + c + 1)
                r = rstd[:, c * TC:(c + 1) * TC]
                steps.then(nc.gpsimd.tensor_scalar(r, meanvar[:, c * TC:(c + 1) * TC, 1], EPS, None, ALU.add))
                steps.wait()
                nc.gpsimd.tensor_tensor(r, r, minus_half[:, 0:TC], ALU.pow).then_inc(rstd_ready, 1)

            def rstd_of(norm):
                for c in range(NC):
                    rstd_of_chunk(norm, c)

            def zero_keys(c):
                nc.gpsimd.memset(ks[:, :, :, chunk(c)].bitcast(F32), 0.0).then_inc(ks_zero, 1)

            rstd_of_chunk(0, 0)
            zero_keys(0)
            for c in range(1, NC):
                rstd_of_chunk(0, c)
            for c in range(1, NC):
                zero_keys(c)
            steps.then(nc.gpsimd.memset(v_aug[:], 1.0))
            steps.wait()
            pool.wait_ge(bo_gated, 1)
            for c in range(NC):
                pool.wait_ge(xn_ready, c + 1)
                xc = x[:, c * TC:(c + 1) * TC, :]
                nc.gpsimd.tensor_tensor(xc, xc, bo[:].rearrange("p (o f) -> p o f", o=1).to_broadcast([P, TC, D]), ALU.add).then_inc(xb_ready, 1)
            def scale_weights():
                pool.wait_ge(weights_in, 16 * N_WEIGHTS)
                for i in range(3):
                    part = eb2_parts[:, 0, :]
                    steps.then(nc.gpsimd.tensor_copy(part, eb2[:]))
                    steps.wait()
                    for k in range(2):
                        rows = choice_rows[:, 3 * k + i:3 * k + i + 1]
                        if i == 0:
                            steps.then(nc.gpsimd.tensor_scalar(eb2_rows[:, k, :], part, rows, None, ALU.mult))
                        else:
                            steps.then(nc.gpsimd.tensor_scalar(eb2_parts[:, 1, :], part, rows, None, ALU.mult))
                            steps.wait()
                            steps.then(nc.gpsimd.tensor_tensor(eb2_rows[:, k, :], eb2_rows[:, k, :], eb2_parts[:, 1, :], ALU.add))
                        steps.wait()
                    if i < 2:
                        steps.then(nc.gpsimd.tensor_tensor(eb2[:], eb2[:], part, ALU.subtract))
                        steps.wait()
                pool.sem_inc(eb2_ready, 1)
                for i in range(2):
                    nc.gpsimd.tensor_tensor(fw2[:, i, :], fw2[:, i, :], iw[:], ALU.mult)
                nc.gpsimd.tensor_tensor(fb2[:], fb2[:], iw[:], ALU.mult).then_inc(fb2_ready, 1)

            for b in range(B):
                if b % BC == 0:
                    pool.wait_ge(v_ready, b // BC + 1)
                if b >= BC:
                    pool.wait_ge(pv_done, GROUPS * (b - BC + 1))
                nc.gpsimd.tensor_copy(v_aug[:, b % BC, :, :, 0:HD], v_all[:, 2 * b:2 * b + 2, :, :]).then_inc(v_aug_ready, 1)
                if b == 1:
                    scale_weights()
                if b > BC and b % BC == 0:
                    rstd_of_chunk(1, b // BC - 2)

            rstd_of_chunk(1, NC - 2)
            rstd_of_chunk(1, NC - 1)
            pool.wait_ge(x1_ready, B)
            nc.gpsimd.memset(route, 0.0).then_inc(route_zero, 1)
            for c in range(NC):
                pool.wait_ge(xn_ready, NC + c + 1)
                pool.wait_ge(xT_psum, NC + c + 1)
                pool.wait_ge(fb2_ready, 1)
                xc = xn[:, c * TC:(c + 1) * TC, :]
                steps.then(nc.gpsimd.tensor_tensor(xc, xc, fb2[:].rearrange("p (o f) -> p o f", o=1).to_broadcast([P, TC, D]), ALU.add))
            pool.wait_ge(chosen_ready, 16)
            for it in range(2):
                for c in range(NC):
                    n = it * NC + c
                    for j in range(4):
                        e = 4 * n + j
                        pool.wait_ge(gelu_done, 5 * n + j + 1)
                        nc.gpsimd.tensor_tensor(hidden[:, 1, j, c, :], unmasked[:, e % 2, :], chosen[:, 1, j, c, :], ALU.mult).then_inc(masked_second, 1)
            rstd_of(2)

            def split_weights(e):
                pool.wait_ge(w_in[e], 48)
                if e >= 2:
                    pool.wait_ge(up_psum, NC * MT * (e - 1))
                steps.then(nc.gpsimd.tensor_copy(w12_hi[:, e % 2, :, :], w12[:, e % 2, :, :]))
                steps.wait()
                nc.gpsimd.tensor_tensor(w12_lo[:, e % 2, :, :], w12[:, e % 2, :, :], w12_hi[:, e % 2, :, :].bitcast(F32),
                                        ALU.subtract).then_inc(w12_ready, 1)

            pool.wait_ge(x2_ready, NC)
            split_weights(0)
            rstd_of(3)
            for c in range(NC):
                pool.wait_ge(xT_ready, 3 * NC + c + 1)
                pool.wait_ge(xT_hi_ready, c + 1)
                nc.gpsimd.tensor_tensor(xT_lo[:, chunk(c)], xT[:, chunk(c)], xT_hi[:, chunk(c)].bitcast(F32), ALU.subtract).then_inc(xT_lo_ready, 1)
            for e in range(1, E):
                split_weights(e)

        @block.scalar
        def _(act):
            for dst, src in ((qk_bias, a["qk_bias"]), (gates, a["gates"]), (bv, a["bv"].partition_broadcast(P)),
                             (bo, a["bo"].partition_broadcast(P)), (wo, a["wo"])):
                act.dma_start(dst[:], src).then_inc(consts_in, 16)
            act.wait_ge(consts_in, 16 * N_CONSTS)
            nc.scalar.activation(tg[:], gates[:], ACT.Tanh).then_inc(tg_ready, 1)
            for c in range(NC):
                act.wait_ge(xT_psum, c + 1)
                nc.scalar.copy(xT[:, chunk(c)], bank[4 * (c % 2)][:]).then_inc(xT_ready, 1)
                act.wait_ge(qkv_psum, c + 1)
                if c == 3:
                    act.wait_ge(stacked_out[0], 96)
                for s in range(2):
                    if c >= 1:
                        act.wait_ge(qk_used, 2 * (c - 1) + s + 1)
                    ps = bank[4 * (c % 2) + 1 + s]
                    nc.scalar.activation(qk[:, s, :], ps[:], ACT.Identity, bias=qk_bias[:, s:s + 1]).then_inc(qk_high, 1)
                    nc.scalar.activation(parts_of[c][:, s, 2, :], ps[:], ACT.Identity, bias=qk_bias[:, s:s + 1]).then_inc(qk_high, 1)
            for b in range(B):
                for h in range(H):
                    if h < 2:
                        act.wait_ge(maxT_psum, 2 * b + h + 1)
                        src = bank[s1[h][0]][:].bitcast(BF16)[96:102, :].rearrange("r (p n) -> r p n", n=S)
                        nc.scalar.copy(qs[96:102, 4 * h:4 * h + 4, b * S:(b + 1) * S], src).then_inc(maxT_ready, 1)
                    g = GROUPS * b + h // 4
                    act.wait_ge(s2_ready, H * b + h + 1)
                    if h == 4 and b == 0:
                        act.wait_ge(stacked_out[2], 96)
                    if h % 4 == 0 and g >= 2:
                        act.wait_ge(pv_done, g - 1)
                    nc.scalar.activation(probs[:, g % 2, h % 4, :, :], s2[h % 2][:].rearrange("p (k q) -> p k q", k=2), ACT.Exp,
                                         scale=float(HD) ** -0.5).then_inc(exp_done, 1)


            act.wait_ge(weights_in, 16 * N_WEIGHTS)
            for c in range(NC):
                act.wait_ge(xT_psum, NC + c + 1)
                nc.scalar.copy(xT[:, chunk(c)], bank[c][:]).then_inc(xT_ready, 1)
            act.wait_ge(x1_ready, B)
            for c in range(NC):
                act.wait_ge(router_psum, c + 1)
                nc.scalar.activation(router_h[:, c, :], bank[4 + c % 2][0:32, :], ACT.Gelu, bias=rb1[:, 0:1]).then_inc(router_h_ready, 1)
            nc.scalar.activation(shared_w[:, 1:2], shared_w[:, 0:1], ACT.Exp, scale=-1.0)
            act.wait_ge(gap_ready, 1)
            nc.scalar.activation(w_first, gap, ACT.Exp).then_inc(exp_gap_ready, 1)
            for c in range(NC):
                act.wait_ge(routeT32_ready, c + 1)
                nc.scalar.copy(routeT[:, c, :], routeT32[:, c, :]).then_inc(routeT_ready, 1)
            for n in range(0, 8 * NC, 2):
                k, j, c = n % 8 // 4, n % 4, n // 8
                act.wait_ge(chosen_psum, n + 1)
                nc.scalar.activation(chosen[:, k, j, c, :], bank[4 + n % 4][:], ACT.Copy, saturate=False).then_inc(chosen_ready, 1)
            for n in range(2 * NC):
                act.wait_ge(weight_psum, n + 1)
                nc.scalar.copy(weight[:, n % 2, n // 2, :], bank[n % 4][:]).then_inc(weight_ready, 1)

            steps = Chain(act, act_step)

            def gelus(it, c):
                n = NC * it + c
                for j in range(4):
                    e = 4 * n + j
                    act.wait_ge(hidden_psum, 5 * n + j + 1)
                    if e >= 2:
                        act.wait_ge(masked_first, e - 1)
                        act.wait_ge(masked_second, e - 1)
                    nc.scalar.activation(unmasked[:, e % 2, :], bank[(5 * n + j) % 2][:], ACT.Gelu, bias=eb1[:, j:j + 1]).then_inc(gelu_done, 1)
                act.wait_ge(hidden_psum, 5 * n + 5)
                nc.scalar.activation(shared_h[:, c, :], bank[(5 * n + 4) % 2][0:96, :], ACT.Gelu, bias=sb1[:, 0:1]).then_inc(gelu_done, 1)

            def softplus(it, c):
                for k in range(3):
                    u = 3 * (NC * it + c) + k
                    act.wait_ge(capped_ready, u + 1)
                    t = soft[:, k, c % 2, :]
                    steps.then(nc.scalar.activation(t, t, ACT.Exp))
                    steps.wait()
                    nc.scalar.activation(t, t, ACT.Ln, bias=1.0).then_inc(ln_done, 1)

            def sigmoids(it, c):
                n = NC * it + c
                if n:
                    act.wait_ge(state_ready, n)
                outs = [(halt, hb2[:, 0:1])] + [(sig_g[:, k, :], sb2[:, 2:3] if k == 0 else 0.0) for k in range(3)]
                if it:
                    outs += [(sig_a[:, k, :], sb2[:, 0:1] if k == 0 else 0.0) for k in range(3)]
                for i, (dst, bias) in enumerate(outs):
                    w = gate_use(it, c) + i
                    act.wait_ge(gate_psum, w + 1)
                    nc.scalar.activation(dst[:] if i == 0 else dst, bank[5 + w % 3][:], ACT.Sigmoid, bias=bias).then_inc(sigmoid_done, 1)

            for it in range(2):
                for c in range(NC):
                    gelus(it, c)
                for c in range(0, NC, 2):
                    nc.scalar.preload_act_table_set("natural_log_exp_and_others")
                    softplus(it, c)
                    softplus(it, c + 1)
                    sigmoids(it, c)
                    sigmoids(it, c + 1)
            for c in range(NC):
                for m in range(2):
                    act.wait_ge(refine_psum, 2 * c + m + 1)
                    if c >= 1 and m == 0:
                        act.wait_ge(refined_psum, c)
                    nc.scalar.activation(w2t[:, m, :], bank[m][:], ACT.Gelu, bias=fb1[:, m:m + 1]).then_inc(refine_h_ready, 1)

            for c in range(NC):
                act.wait_ge(xT_psum, 2 * NC + c + 1)
                nc.scalar.copy(xT[:, chunk(c)], bank[4 + c][:]).then_inc(xT_ready, 1)
            for b in range(B + 1):
                if b < B:
                    act.wait_ge(negmax2_ready, b + 1)
                    if b >= 2:
                        act.wait_ge(probsT_psum, b - 1)
                    for q in range(2):
                        last = nc.scalar.activation(probs2[:, b % 2, q, :], bank[b % 2][:, q * S:(q + 1) * S], ACT.Exp,
                                                    bias=negmax2[:, b, q:q + 1], accum_out=sums2[:, b, q:q + 1])
                    last.then_inc(exp2_done, 1)
                if b > 0:
                    act.wait_ge(probsT_psum, b)
                    if b >= 3:
                        act.wait_ge(fused_psum, b - 2)
                    nc.scalar.copy(probsT[:, (b - 1) % 2, :, :].rearrange("p k q -> p (k q)"), bank[2 + (b - 1) % 2][:]).then_inc(probsT_ready, 1)

            for c in range(NC):
                act.wait_ge(xT_psum, 3 * NC + c + 1)
                nc.scalar.copy(xT[:, chunk(c)], bank[c][:]).then_inc(xT_ready, 1)
            for c in range(NC):
                nc.scalar.copy(xT_hi[:, chunk(c)], bank[c][:]).then_inc(xT_hi_ready, 1)
            act.wait_ge(gap2_ready, 1)
            nc.scalar.activation(w_top[:, 1, :], gap2[:], ACT.Exp).then_inc(w2nd_ready, 1)
            for c in range(NC):
                act.wait_ge(shareT_psum, c + 1)
                nc.scalar.copy(shareT[:, c, :], bank[4 + c % 2][0:E, :]).then_inc(shareT_ready, 1)
            for n in range(E * NC * MT):
                e, m = n // (NC * MT), n % MT
                act.wait_ge(up_psum, n + 1)
                if n >= 2:
                    act.wait_ge(gated_ready, n - 1)
                nc.scalar.activation(silu_g[:, n % 2, :], bank[2 * (n % 2)][:], ACT.Silu, bias=b12[:, 0, e, m:m + 1]).then_inc(silu_done, 1)

        @block.vector
        def _(dve):
            steps = Chain(dve, dve_step)

            def layer_norm_stats(c):
                for t in range(c * TC, (c + 1) * TC):
                    steps.then(nc.vector.bn_stats(stats[:, t, :], x[:, t, :]))
                steps.wait()
                for t in range(c * TC, (c + 1) * TC):
                    last = nc.vector.bn_aggr(meanvar[:, t, :], stats[:, t, :])
                last.then_inc(stats_ready, 1)

            def layer_norm_apply(c, n):
                dve.wait_ge(rstd_ready, n)
                for t in range(c * TC, (c + 1) * TC):
                    last = nc.vector.tensor_scalar(xn[:, t, :], x[:, t, :], meanvar[:, t, 0:1], rstd[:, t:t + 1],
                                                   ALU.subtract, ALU.mult)
                last.then_inc(xn_ready, 1)

            for c in range(NC):
                dve.wait_ge(x_in[c], 16)
                layer_norm_stats(c)
                if c == 0:
                    layer_norm_apply(0, 1)
            for c in range(1, NC):
                layer_norm_apply(c, c + 1)
            dve.wait_ge(consts_in, 16 * N_CONSTS)
            steps.then(nc.vector.tensor_copy(identb[:], ident[:]))
            dve.wait_ge(tg_ready, 1)
            nc.vector.tensor_scalar(bo[:], bo[:], tg[:, 0:1], None, ALU.mult).then_inc(bo_gated, 1)
            for c in range(NC):
                dve.wait_ge(qkv_psum, c + 1)
                vb = bank[4 * (c % 2) + 3][:].rearrange("p (t f) -> p t f", f=D)
                nc.vector.tensor_tensor(v_all[:, c * TC:(c + 1) * TC].rearrange("p t h d -> p t (h d)"), vb,
                                        bv[:].rearrange("p (o f) -> p o f", o=1).to_broadcast([P, TC, D]), ALU.add).then_inc(v_ready, 1)
                for s in range(2):
                    pc = parts_of[c][:, s]
                    dve.wait_ge(qk_high, 4 * c + 2 * s + 2)
                    nc.vector.tensor_tensor(rest[:, s, :], qk[:, s, :], pc[:, 2, :], ALU.subtract).then_inc(qk_used, 1)
                    dve.wait_ge(qk_used, 2 * c + s + 1)
                    steps.then(nc.vector.tensor_copy(pc[:, 1, :], rest[:, s, :]))
                    steps.wait()
                    last = nc.vector.tensor_tensor(pc[:, 0, :], rest[:, s, :], pc[:, 1, :], ALU.subtract)
                    if s == 0:
                        steps.then(last)
                last.then_inc(parts_ready, 1)

            def maxima(b, p):
                n = PAIRS * b + p
                dve.wait_ge(s1_ready, n + 1)
                i, j = s1[n % 2]
                for h, bk in enumerate((i, j)):
                    last = nc.vector.tensor_reduce(negmax[:, p, h, :], bank[bk][:].rearrange("p (q k) -> p q k", q=2), AX.X, ALU.max, negate=True)
                last.then_inc(max_done, 1)

            def split_maxima(b):
                dve.wait_ge(max_done, PAIRS * (b + 1))
                if b:
                    dve.wait_ge(maxT_psum, 2 * b)
                hi, mid, lo = (max_parts[:, :, :, :, i].rearrange("p q r h -> p r h q") for i in range(3))
                steps.then(nc.vector.tensor_copy(hi, negmax[:]))
                steps.wait()
                steps.then(nc.vector.tensor_tensor(max_rest[:], negmax[:], hi, ALU.subtract))
                steps.wait()
                steps.then(nc.vector.tensor_copy(mid, max_rest[:]))
                steps.wait()
                nc.vector.tensor_tensor(lo, max_rest[:], mid, ALU.subtract).then_inc(max_parts_ready, 1)

            def normalise(b, half):
                n = 2 * b + half
                dve.wait_ge(pv_done, GROUPS * b + 2 * half + 2)
                if b >= 2 and half == 0:
                    dve.wait_ge(y_psum, b - 1)
                if n == 0:
                    dve.wait_ge(stacked_out[1], 96)
                if n:
                    dve.wait_ge(attn_ready, n)
                steps.then(nc.vector.transpose(sumsT[:].rearrange("p i r -> p (i r)"), o[half][:]))
                steps.wait()
                steps.then(nc.vector.reciprocal(recip[:], sumsT[:, :, HD]))
                steps.wait()
                steps.then(nc.vector.transpose(recips[:].rearrange("p a q -> p (a q)"), recip[:].rearrange("p (i o) -> p i o", o=1).to_broadcast([P, CH // 32, 32])))
                steps.wait()
                nc.vector.tensor_tensor(attnT[:, b % BC, 2 * half:2 * half + 2, :], o[half][:].rearrange("p (a q) -> p a q", a=2),
                                        recips[:], ALU.mult).then_inc(attn_ready, 1)

            def residual(b):
                dve.wait_ge(y_psum, b + 1)
                if b % BC == 0:
                    dve.wait_ge(xb_ready, b // BC + 1)
                xb = x[:, 2 * b:2 * b + 2, :].rearrange("p t f -> p (t f)")
                nc.vector.scalar_tensor_tensor(xb, s2[0][:, 0:2 * D], tg[:, 0:1], xb, ALU.mult, ALU.add).then_inc(x1_ready, 1)

            for p in range(PAIRS):
                maxima(0, p)
            split_maxima(0)
            for b in range(B):
                for p in range(PAIRS):
                    if p == 4 and b > 0:
                        residual(b - 1)
                    if b > 1 and b % BC == 1:
                        if p == 1:
                            dve.wait_ge(x1_ready, b - 1)
                            layer_norm_stats(b // BC - 1)
                        if p == 4:
                            layer_norm_apply(b // BC - 1, NC + b // BC)
                    if b + 1 < B:
                        maxima(b + 1, p)
                if b + 1 < B:
                    split_maxima(b + 1)
                normalise(b, 0)
                normalise(b, 1)
            residual(B - 1)

            dve.wait_ge(x1_ready, B)
            layer_norm_stats(NC - 1)
            layer_norm_apply(NC - 1, 2 * NC)
            dve.wait_ge(logits_psum, 1)
            dve.wait_ge(weights_in, 16 * N_WEIGHTS)
            steps.then(nc.vector.tensor_tensor(logits, bank[6][:, 0:NT * E].rearrange("p (t e) -> p t e", e=E),
                                               rb2[:].rearrange("p (o e) -> p o e", o=1).to_broadcast([P, NT, E]), ALU.add))
            steps.wait()
            for t in range(NT):
                steps.then(nc.vector.max(top[:, t, :], logits[:, t, :]))
            steps.wait()
            for t in range(NT):
                steps.then(nc.vector.max_index(top_at[:, t, :], top[:, t, :], logits[:, t, :]))
            nc.vector.tensor_tensor(gap, top[:, :, 1], top[:, :, 0], ALU.subtract).then_inc(gap_ready, 1)
            steps.wait()
            steps.then(nc.vector.tensor_copy(top_atf, top_at[:, :, 0:2]))
            steps.wait()
            dve.wait_ge(route_zero, 1)
            for k in range(2):
                nc.vector.tensor_tensor(route[:, :, 32 * k:32 * k + 24], iota24[:].rearrange("p (o e) -> p o e", o=1).to_broadcast([P, NT, 24]),
                                        top_atf[:, :, k:k + 1].to_broadcast([P, NT, 24]), ALU.is_equal)
            dve.wait_ge(exp_gap_ready, 1)
            steps.then(nc.vector.tensor_scalar(shared_w[:, 2:3], shared_w[:, 1:2], 1.0, None, ALU.add))
            steps.then(nc.vector.tensor_scalar(gap, w_first, 1.0, None, ALU.add))
            steps.wait()
            steps.then(nc.vector.reciprocal(shared_w[:, 2:3], shared_w[:, 2:3]))
            steps.then(nc.vector.reciprocal(gap, gap))
            steps.wait()
            steps.then(nc.vector.tensor_tensor(shared_w[:, 3:4], shared_w[:, 2:3], shared_w[:, 1:2], ALU.mult))
            steps.wait()
            steps.then(nc.vector.tensor_scalar(route[:, :, 64], gap, shared_w[:, 3:4], None, ALU.mult))
            steps.wait()
            nc.vector.tensor_tensor(route[:, :, 96], route[:, :, 64], w_first, ALU.mult).then_inc(route_ready, 1)
            for c in range(NC):
                dve.wait_ge(routeT_psum, c + 1)
                nc.vector.tensor_copy(routeT32[:, c, :], bank[c][:]).then_inc(routeT32_ready, 1)
            for n in range(1, 8 * NC, 2):
                k, j, c = n % 8 // 4, n % 4, n // 8
                dve.wait_ge(chosen_psum, n + 1)
                nc.vector.tensor_copy(chosen[:, k, j, c, :], bank[4 + n % 4][:], saturate=False).then_inc(routeT32_ready, 1)
            dve.wait_ge(chosen_ready, 4 * NC)
            dve.wait_ge(weight_psum, 2 * NC)

            def mask_first(it, c):
                for j in range(4):
                    e = 4 * (NC * it + c) + j
                    dve.wait_ge(gelu_done, 5 * (NC * it + c) + j + 1)
                    nc.vector.tensor_tensor(hidden[:, 0, j, c, :], unmasked[:, e % 2, :], chosen[:, 0, j, c, :], ALU.mult).then_inc(masked_first, 1)

            def softplus(it, c):
                def capped(k):
                    u = 3 * (NC * it + c) + k
                    dve.wait_ge(soft_psum, u + 1)
                    nc.vector.tensor_scalar(soft[:, k, c % 2, :], bank[2 + u % 3][:], sb2[:, 1:2] if k == 0 else 0.0, CAP,
                                            ALU.add, ALU.min).then_inc(capped_ready, 1)

                def uncapped(k):
                    u = 3 * (NC * it + c) + k
                    dve.wait_ge(ln_done, u + 1)
                    t = soft[:, k, c % 2, :]
                    nc.vector.scalar_tensor_tensor(t, bank[2 + u % 3][:], sb2[:, 1:2] if k == 0 else 0.0, t, ALU.add, ALU.max).then_inc(soft_done, 1)

                capped(0)
                capped(1)
                uncapped(0)
                capped(2)
                uncapped(1)
                uncapped(2)

            def scale_first(c):
                s = [soft[:, k, c % 2, :] for k in range(3)]
                dve.wait_ge(soft_done, 3 * c + 3)
                steps.then(nc.vector.tensor_scalar(s[0], s[0], shared_w[:, 2:3], None, ALU.mult))
                steps.then(nc.vector.tensor_tensor(s[1], s[1], weight[:, 0, c, :], ALU.mult))
                steps.then(nc.vector.tensor_tensor(s[2], s[2], weight[:, 1, c, :], ALU.mult))

            def first_step(c):
                s = [soft[:, k, c % 2, :] for k in range(3)]
                t = [w1t[:, k, :] for k in range(3)]
                xc, vc, u = xT[:, chunk(c)], v[:, c, :], w2t[:, 0, :]
                dve.wait_ge(sigmoid_done, gate_use(0, c) + 1)
                steps.wait()
                steps.then(nc.vector.scalar_tensor_tensor(u, xc, mu[:, 0:1], halt[:], ALU.subtract, ALU.mult))
                dve.wait_ge(sigmoid_done, gate_use(0, c) + 2)
                steps.then(nc.vector.tensor_tensor(t[0], s[0], sig_g[:, 0, :], ALU.mult))
                steps.wait()
                steps.then(nc.vector.tensor_tensor(s[0], s[0], s[1], ALU.add))
                steps.wait()
                steps.then(nc.vector.tensor_tensor(s[0], s[0], s[2], ALU.add))
                steps.wait()
                steps.then(nc.vector.scalar_tensor_tensor(vc, s[0], -1.0, u, ALU.mult, ALU.mult))
                for k in range(1, 3):
                    dve.wait_ge(sigmoid_done, gate_use(0, c) + 2 + k)
                    steps.then(nc.vector.tensor_tensor(t[k], s[k], sig_g[:, k, :], ALU.mult))
                    steps.wait()
                    steps.then(nc.vector.tensor_tensor(t[0], t[0], t[k], ALU.add))
                    steps.wait()
                steps.then(nc.vector.scalar_tensor_tensor(t[0], t[0], -DT, u, ALU.mult, ALU.mult))
                steps.wait()
                nc.vector.tensor_tensor(xc, xc, t[0], ALU.add).then_inc(state_ready, 1)

            def scale_second(c):
                dve.wait_ge(soft_done, 3 * (NC + c) + 3)
                for k in range(3):
                    sk = soft[:, k, c % 2, :]
                    steps.then(nc.vector.scalar_tensor_tensor(sk, xT[:, chunk(c)], mu[:, 0:1], sk, ALU.subtract, ALU.mult))

            def second_step(c):
                s = [soft[:, k, c % 2, :] for k in range(3)]
                t = [w1t[:, k, :] for k in range(3)]
                xc, vc = xT[:, chunk(c)], v[:, c, :]
                for k in range(3):
                    dve.wait_ge(sigmoid_done, gate_use(1, c) + 2 + k)
                    gate = sig_g[:, k, :]
                    if k == 0:
                        steps.then(nc.vector.tensor_scalar(gate, gate, shared_w[:, 2:3], None, ALU.mult))
                    else:
                        steps.then(nc.vector.tensor_tensor(gate, gate, weight[:, k - 1, c, :], ALU.mult))
                for k in range(3):
                    dve.wait_ge(sigmoid_done, gate_use(1, c) + 5 + k)
                    steps.then(nc.vector.tensor_tensor(t[k], vc, sig_a[:, k, :], ALU.mult))
                    steps.wait()
                    steps.then(nc.vector.tensor_tensor(t[k], t[k], s[k], ALU.subtract))
                    steps.wait()
                    steps.then(nc.vector.tensor_tensor(t[k], t[k], sig_g[:, k, :], ALU.mult))
                    steps.wait()
                    if k:
                        steps.then(nc.vector.tensor_tensor(t[0], t[0], t[k], ALU.add))
                        steps.wait()
                steps.then(nc.vector.scalar_tensor_tensor(t[0], t[0], DT, halt[:], ALU.mult, ALU.mult))
                steps.wait()
                nc.vector.tensor_tensor(xc, xc, t[0], ALU.add).then_inc(state_ready, 1)

            for it in range(2):
                for c in range(NC):
                    mask_first(it, c)
                for c in range(0, NC, 2):
                    for d in (c, c + 1):
                        softplus(it, d)
                        (scale_second if it else scale_first)(d)
                    for d in (c, c + 1):
                        (second_step if it else first_step)(d)
            for c in range(NC):
                xc = x[:, c * TC:(c + 1) * TC, :].rearrange("p t f -> p (t f)")
                base = xn[:, c * TC:(c + 1) * TC, :].rearrange("p t f -> p (t f)")
                steps.then(nc.vector.scalar_tensor_tensor(xc, base, tg[:, 2:3], xc, ALU.mult, ALU.add))
                steps.wait()
                dve.wait_ge(refined_psum, c + 1)
                nc.vector.scalar_tensor_tensor(xc, bank[2 + c % 2][:], tg[:, 2:3], xc, ALU.mult, ALU.add).then_inc(x2_ready, 1)
                dve.wait_ge(x2_ready, c + 1)
                layer_norm_stats(c)
                if c:
                    layer_norm_apply(c - 1, 2 * NC + c)

            layer_norm_apply(NC - 1, 3 * NC)

            def fuse(b):
                dve.wait_ge(exp2_done, b + 1)
                steps.then(nc.vector.reciprocal(sums2[:, b, :], sums2[:, b, :]))
                steps.wait()
                steps.then(nc.vector.tensor_scalar(sums2[:, b, :], sums2[:, b, :], tg[:, 1:2], None, ALU.mult))
                steps.wait()
                dve.wait_ge(fused_psum, b + 1)
                for q in range(2):
                    xt = x[:, 2 * b + q, :]
                    last = nc.vector.scalar_tensor_tensor(xt, bank[4 + b % 2][:, q * D:(q + 1) * D], sums2[:, b, q:q + 1], xt, ALU.mult, ALU.add)
                last.then_inc(x3_ready, 1)

            for b in range(B + 2):
                if b < B:
                    dve.wait_ge(scores_psum, b + 1)
                    nc.vector.tensor_reduce(negmax2[:, b, :], bank[b % 2][:].rearrange("p (q k) -> p q k", q=2), AX.X, ALU.max,
                                            negate=True).then_inc(negmax2_ready, 1)
                if b > 1:
                    fuse(b - 2)
                    if b % BC == 1:
                        dve.wait_ge(x3_ready, b - 1)
                        layer_norm_stats(b // BC - 1)
                    if b % BC == 0 and b > BC:
                        dve.wait_ge(xT_psum, 3 * NC)
                        layer_norm_apply(b // BC - 2, 3 * NC + b // BC - 1)

            layer_norm_apply(NC - 1, 4 * NC)
            dve.wait_ge(small2_in, 16 * 5)
            dve.wait_ge(logits2_psum, 1)
            steps.then(nc.vector.tensor_tensor(logits2[:], bank[6][:, 0:NT * E].rearrange("p (t e) -> p t e", e=E),
                                               br[:].rearrange("p (o e) -> p o e", o=1).to_broadcast([P, NT, E]), ALU.add))
            steps.wait()
            for t in range(NT):
                steps.then(nc.vector.max(top2[:, t, :], logits2[:, t, :]))
            steps.wait()
            for t in range(NT):
                steps.then(nc.vector.max_index(top2_at[:, t, :], top2[:, t, :], logits2[:, t, :]))
            nc.vector.tensor_tensor(gap2[:], top2[:, :, 1], top2[:, :, 0], ALU.subtract).then_inc(gap2_ready, 1)
            steps.wait()
            steps.then(nc.vector.tensor_copy(top2_atf[:], top2_at[:, :, 0:2]))
            steps.wait()
            for k in range(2):
                steps.then(nc.vector.tensor_tensor(is_top[:, k, :, :], iota8[:].rearrange("p (o e) -> p o e", o=1).to_broadcast([P, NT, E]),
                                                   top2_atf[:, :, k:k + 1].to_broadcast([P, NT, E]), ALU.is_equal))
            dve.wait_ge(w2nd_ready, 1)
            steps.then(nc.vector.tensor_scalar(gap2[:], w_top[:, 1, :], 1.0, None, ALU.add))
            steps.wait()
            steps.then(nc.vector.reciprocal(gap2[:], gap2[:]))
            steps.wait()
            steps.then(nc.vector.tensor_scalar(w_top[:, 0, :], gap2[:], tg[:, 3:4], None, ALU.mult))
            steps.wait()
            steps.then(nc.vector.tensor_tensor(w_top[:, 1, :], w_top[:, 1, :], w_top[:, 0, :], ALU.mult))
            steps.wait()
            for k in range(2):
                steps.then(nc.vector.tensor_tensor(is_top[:, k, :, :], is_top[:, k, :, :],
                                                   w_top[:, k, :].rearrange("p (t o) -> p t o", o=1).to_broadcast([P, NT, E]), ALU.mult))
            steps.wait()
            nc.vector.tensor_tensor(share[:], is_top[:, 0, :, :], is_top[:, 1, :, :], ALU.add).then_inc(share_ready, 1)
            for c in range(NC):
                dve.wait_ge(bias3_psum, c + 1)
                xc = x[:, c * TC:(c + 1) * TC, :].rearrange("p t f -> p (t f)")
                nc.vector.tensor_tensor(xc, xc, bank[6 + c % 2][:], ALU.add).then_inc(bias3_added, 1)

            dve.wait_ge(share_ready, 1)
            dve.wait_ge(bias3_added, NC)

            def add_expert(k):
                e, c = k // NC, k % NC
                dve.wait_ge(down_psum, k + 1)
                if k >= NC:
                    dve.wait_ge(added, k - NC + 1)
                for t in range(TC):
                    xt = x[:, c * TC + t, :]
                    last = nc.vector.scalar_tensor_tensor(xt, bank[4 + k % 2][:, t * D:(t + 1) * D], share[:, c * TC + t, e:e + 1], xt,
                                                          ALU.mult, ALU.add)
                last.then_inc(added, 1)

            for n in range(E * NC * MT):
                e, k, m = n // (NC * MT), n // MT, n % MT
                dve.wait_ge(silu_done, n + 1)
                if k >= 2 and m == 0:
                    dve.wait_ge(down_psum, k - 1)
                nc.vector.scalar_tensor_tensor(gated[:, k % 2, m, :], bank[2 * (n % 2) + 1][:], b12[:, 1, e, m:m + 1], silu_g[:, n % 2, :],
                                               ALU.add, ALU.mult).then_inc(gated_ready, 1)
                if m == 1 and k > 0:
                    add_expert(k - 1)
            add_expert(E * NC - 1)

        @block.tensor
        def _(pe):
            pe.wait_ge(consts_in, 16 * N_CONSTS)
            for c in range(NC):
                bk = [bank[4 * (c % 2) + i] for i in range(4)]
                pe.wait_ge(xn_ready, c + 1)
                if c >= 2:
                    pe.wait_ge(qk_high, 4 * (c - 1))
                    pe.wait_ge(v_ready, c - 1)
                for t in range(TC):
                    last = nc.tensor.transpose(bk[0][:, t * P:(t + 1) * P], xn[:, c * TC + t, :], ident[:])
                last.then_inc(xT_psum, 1)
                if c == 0:
                    pe.wait_ge(ctx_in, 16)
                nc.tensor.matmul(bk[2][:], wkT[:], ctxT[:, chunk(c)], start=True, stop=True)
                for t in range(TC):
                    n = (c * TC + t) * P
                    nc.tensor.matmul(bk[3][:, t * D:(t + 1) * D], ctxT[:, n:n + P], wvT[:], start=True, stop=True)
                pe.wait_ge(xT_ready, c + 1)
                nc.tensor.matmul(bk[1][:], wqT[:], xT[:, chunk(c)], start=True, stop=True).then_inc(qkv_psum, 1)

            def scores_by_query(b, p):
                n = PAIRS * b + p
                if n >= 2:
                    pe.wait_ge(max_done, n - 1)
                for h in range(2):
                    for q in range(2):
                        last = nc.tensor.matmul(bank[s1[n % 2][h]][:, q * S:(q + 1) * S],
                                                qs[0:96, p, b * S + q * P:b * S + (q + 1) * P],
                                                ks[0:96, p, h, b * S:(b + 1) * S], start=True, stop=True)
                last.then_inc(s1_ready, 1)

            def transpose_maxima(b, half):
                if half == 0:
                    pe.wait_ge(max_parts_ready, b + 1)
                dst = bank[s1[half][0]][:].bitcast(BF16)
                for i in range(4):
                    for q in range(2):
                        last = nc.tensor.transpose(dst[96:102, i * S + q * P:i * S + (q + 1) * P],
                                                   max_parts[:, q, 4 * half + i, :, :].rearrange("p h r -> p (h r)"), identb[:])
                last.then_inc(maxT_psum, 1)

            def scores_by_key(b, h):
                n = H * b + h
                if n >= 2:
                    pe.wait_ge(exp_done, n - 1)
                for k in range(2):
                    last = nc.tensor.matmul(s2[h % 2][:, k * S:(k + 1) * S],
                                            ks[0:102, h // 2, h % 2, b * S + k * P:b * S + (k + 1) * P],
                                            qs[0:102, h // 2, b * S:(b + 1) * S], start=True, stop=True)
                last.then_inc(s2_ready, 1)

            def weigh_values(b, g):
                pe.wait_ge(exp_done, H * b + 4 * g + 4)
                if g % 2 == 0 and b:
                    pe.wait_ge(attn_ready, 2 * (b - 1) + g // 2 + 1)
                for k in range(2):
                    for j in range(4):
                        last = nc.tensor.matmul(o[g // 2][32 * j:32 * j + 32, (g % 2) * S:(g % 2 + 1) * S],
                                                v_aug[:, b % BC, k, 4 * g + j, :], probs[:, g % 2, j, k, :],
                                                start=(k == 0), stop=(k == 1), skip_group_check=True)
                last.then_inc(pv_done, 1)

            def project(b):
                pe.wait_ge(attn_ready, 2 * b + 2)
                for q in range(2):
                    for g in range(GROUPS):
                        last = nc.tensor.matmul(s2[0][:, q * D:(q + 1) * D], attnT[:, b % BC, g, q * P:(q + 1) * P], wo[:, g, :],
                                                start=(g == 0), stop=(g == GROUPS - 1))
                last.then_inc(y_psum, 1)

            pe.wait_ge(qk_high, 4 * NC)
            pe.wait_ge(v_ready, NC)
            pe.wait_ge(stacks_in[0], 96)
            for p in range(PAIRS):
                scores_by_query(0, p)
            for b in range(B):
                transpose_maxima(b, 0)
                transpose_maxima(b, 1)
                if b:
                    weigh_values(b - 1, GROUPS - 1)
                if (b + 1) % BC == 0 and b + 1 < B:
                    pe.wait_ge(stacks_in[(b + 1) // BC], 96)
                pe.wait_ge(v_aug_ready, b + 1)
                for h in range(H):
                    if h in (0, 3, H // 2):
                        pe.wait_ge(maxT_ready, 2 * b + 1 + (h > 0))
                    if h == 8 and b > 0:
                        pe.wait_ge(exp_done, H * b + 7)
                        project(b - 1)
                        pe.wait_ge(x1_ready, b)
                    scores_by_key(b, h)
                    if h in NEXT_PAIR_AFTER and b + 1 < B:
                        scores_by_query(b + 1, NEXT_PAIR_AFTER.index(h))
                    if h % 4 == 1 and h > 4:
                        weigh_values(b, h // 4 - 1)
            weigh_values(B - 1, GROUPS - 1)

            def transpose_chunk(c, norm, first):
                pe.wait_ge(xn_ready, NC * norm + c + 1)
                for t in range(TC):
                    last = nc.tensor.transpose(bank[first + c][:, t * P:(t + 1) * P], xn[:, c * TC + t, :], ident[:])
                last.then_inc(xT_psum, 1)

            pe.wait_ge(max_done, PAIRS * B)
            for c in range(NC - 1):
                transpose_chunk(c, 1, 0)
            project(B - 1)

            pe.wait_ge(weights_in, 16 * N_WEIGHTS)
            pe.wait_ge(x1_ready, B)
            transpose_chunk(NC - 1, 1, 0)
            for c in range(NC):
                pe.wait_ge(xT_ready, NC + c + 1)
                if c >= 2:
                    pe.wait_ge(router_h_ready, c - 1)
                nc.tensor.matmul(bank[4 + c % 2][0:32, :], rw1[:], xT[:, chunk(c)], start=True, stop=True).then_inc(router_psum, 1)
            for c in range(NC):
                pe.wait_ge(router_h_ready, c + 1)
                for t in range(TC):
                    n = c * TC + t
                    last = nc.tensor.matmul(bank[6][:, n * E:(n + 1) * E], router_h[:, c, t * P:(t + 1) * P], rw2[:], start=True, stop=True)
            last.then_inc(logits_psum, 1)
            pe.wait_ge(route_ready, 1)
            pe.wait_ge(selectors_in, 32)
            for c in range(NC):
                for t in range(TC):
                    last = nc.tensor.transpose(bank[c][:, t * P:(t + 1) * P], route[:, c * TC + t, :], ident[:])
                last.then_inc(routeT_psum, 1)
            for n in range(8 * NC):
                k, j, c = n % 8 // 4, n % 4, n // 8
                pe.wait_ge(routeT_ready, c + 1)
                if n >= 4 and n % 2 == 0:
                    pe.wait_ge(chosen_ready, n // 2 - 1)
                if n >= 4 and n % 2 == 1:
                    pe.wait_ge(routeT32_ready, NC + n // 2 - 1)
                nc.tensor.matmul(bank[4 + n % 4][:], choice_sel[:, k, j, :], routeT[:, c, :], start=True, stop=True).then_inc(chosen_psum, 1)
            pe.wait_ge(routeT_ready, NC)
            pe.wait_ge(routeT32_ready, NC)
            for n in range(2 * NC):
                if n >= 4:
                    pe.wait_ge(weight_ready, n - 3)
                nc.tensor.matmul(bank[n % 4][:], weight_sel[:, n % 2, :], routeT32[:, n // 2, :], start=True, stop=True).then_inc(weight_psum, 1)

            pe.wait_ge(weight_ready, 2 * NC)
            pe.wait_ge(chosen_ready, 4 * NC)
            pe.wait_ge(routeT32_ready, NC + 4 * NC)
            pe.wait_ge(eb2_ready, 1)

            def hidden_units(it, c):
                n = NC * it + c
                if it:
                    pe.wait_ge(state_ready, c + 1)
                for j in range(5):
                    m = 5 * n + j
                    if m >= 2:
                        pe.wait_ge(gelu_done, m - 1)
                    if j < 4:
                        w, dst = ew1[:, :, j * P:(j + 1) * P], bank[m % 2][:]
                    else:
                        w, dst = sw1, bank[m % 2][0:96, :]
                    last = nc.tensor.matmul(dst, w[:, 0, :], xT[:, chunk(c)], start=True, stop=not it)
                    if it:
                        last = nc.tensor.matmul(dst, w[:, 1, :], v[:, c, :], start=False, stop=True)
                    last.then_inc(hidden_psum, 1)

            def controller(dst, k, part, c):
                cols = slice(part * D, (part + 1) * D)
                if k == 0:
                    return nc.tensor.matmul(dst, sw2[:, cols], shared_h[:, c, :], start=True, stop=True)
                nc.tensor.matmul(dst, eb2_rows[:, k - 1, cols], routeT[:, c, :], start=True, stop=False)
                for j in range(4):
                    last = nc.tensor.matmul(dst, ew2[:, j, cols], hidden[:, k - 1, j, c, :], start=False, stop=(j == 3))
                return last

            def soft_parts(it, c):
                n = NC * it + c
                pe.wait_ge(gelu_done, 5 * n + 5)
                pe.wait_ge(masked_first, 4 * n + 4)
                pe.wait_ge(masked_second, 4 * n + 4)
                for k in range(3):
                    u = 3 * n + k
                    if u >= 3:
                        pe.wait_ge(soft_done, u - 2)
                    controller(bank[2 + u % 3][:], k, 1, c).then_inc(soft_psum, 1)

            def gate_parts(it, c):
                for i in range(7 if it else 4):
                    w = gate_use(it, c) + i
                    if w >= 3:
                        pe.wait_ge(sigmoid_done, w - 2)
                    dst = bank[5 + w % 3][:]
                    if i == 0:
                        last = nc.tensor.matmul(dst, hw2[:], shared_h[:, c, :], start=True, stop=True)
                    else:
                        last = controller(dst, (i - 1) % 3, 2 if i < 4 else 0, c)
                    last.then_inc(gate_psum, 1)

            for it in range(2):
                for c in range(NC):
                    hidden_units(it, c)
                for c in range(0, NC, 2):
                    soft_parts(it, c)
                    soft_parts(it, c + 1)
                    gate_parts(it, c)
                    gate_parts(it, c + 1)
            pe.wait_ge(fb2_ready, 1)
            for c in range(NC):
                pe.wait_ge(state_ready, NC + c + 1)
                if c == 0:
                    pe.wait_ge(soft_done, 6 * NC)
                for m in range(2):
                    if c:
                        pe.wait_ge(refine_h_ready, 2 * (c - 1) + m + 1)
                    nc.tensor.matmul(bank[m][:], fw1[:, m * P:(m + 1) * P], xT[:, chunk(c)], start=True, stop=True).then_inc(refine_psum, 1)
                pe.wait_ge(refine_h_ready, 2 * c + 2)
                if c >= 2:
                    pe.wait_ge(x2_ready, c - 1)
                for t in range(TC):
                    for m in range(2):
                        last = nc.tensor.matmul(bank[2 + c % 2][:, t * D:(t + 1) * D], w2t[:, m, t * P:(t + 1) * P], fw2[:, m, :],
                                                start=(m == 0), stop=(m == 1))
                last.then_inc(refined_psum, 1)

            pe.wait_ge(soft_done, 6 * NC)
            pe.wait_ge(sigmoid_done, gate_use(1, NC))
            for c in range(NC):
                transpose_chunk(c, 2, 4)
            pe.wait_ge(xT_ready, 3 * NC)
            pe.wait_ge(ctx2_in, 16 * (NC + 1))
            pe.wait_ge(x2_ready, NC)
            pe.wait_ge(refine_h_ready, 2 * NC)
            for b in range(B + 2):
                if b < B:
                    if b >= 2:
                        pe.wait_ge(exp2_done, b - 1)
                    for q in range(2):
                        last = nc.tensor.matmul(bank[b % 2][:, q * S:(q + 1) * S], xT[:, (2 * b + q) * P:(2 * b + q + 1) * P],
                                                ctxT2[:, b * S:(b + 1) * S], start=True, stop=True)
                    last.then_inc(scores_psum, 1)
                if 0 < b <= B:
                    d = b - 1
                    pe.wait_ge(exp2_done, d + 1)
                    if d >= 2:
                        pe.wait_ge(probsT_ready, d - 1)
                    for k in range(2):
                        for q in range(2):
                            last = nc.tensor.transpose(bank[2 + d % 2][:, k * S + q * P:k * S + (q + 1) * P],
                                                       probs2[:, d % 2, q, k * P:(k + 1) * P], ident[:])
                    last.then_inc(probsT_psum, 1)
                if b > 1:
                    d = b - 2
                    pe.wait_ge(probsT_ready, d + 1)
                    if d >= 2:
                        pe.wait_ge(x3_ready, d - 1)
                    for q in range(2):
                        for k in range(2):
                            last = nc.tensor.matmul(bank[4 + d % 2][:, q * D:(q + 1) * D], probsT[:, d % 2, k, q * P:(q + 1) * P],
                                                    ctxm[:, 2 * d + k, :], start=(k == 0), stop=(k == 1))
                    last.then_inc(fused_psum, 1)

            pe.wait_ge(probsT_ready, B)
            pe.wait_ge(small2_in, 16 * 5)
            for c in range(NC):
                transpose_chunk(c, 3, 0)
            for c in range(NC):
                pe.wait_ge(xT_ready, 3 * NC + c + 1)
                for t in range(TC):
                    n = c * TC + t
                    last = nc.tensor.matmul(bank[6][:, n * E:(n + 1) * E], xT[:, n * P:(n + 1) * P], wr[:], start=True, stop=True)
            last.then_inc(logits2_psum, 1)
            def up(n):
                e, k, m = n // (NC * MT), n // MT, n % MT
                if n % (NC * MT) == 0:
                    pe.wait_ge(w12_ready, e + 1)
                if n < NC * MT and m == 0:
                    pe.wait_ge(xT_hi_ready, NC)
                    pe.wait_ge(xT_lo_ready, k + 1)
                if n >= 2:
                    pe.wait_ge(gated_ready, n - 1)
                cols, xc = slice(m * P, (m + 1) * P), chunk(k % NC)
                for i in range(2):
                    dst, w_hi, w_lo = bank[2 * (n % 2) + i][:], w12_hi[:, e % 2, i, cols], w12_lo[:, e % 2, i, cols]
                    nc.tensor.matmul(dst, w_hi, xT_hi[:, xc], start=True, stop=False)
                    nc.tensor.matmul(dst, w_hi, xT_lo[:, xc], start=False, stop=False)
                    last = nc.tensor.matmul(dst, w_lo, xT_hi[:, xc], start=False, stop=True)
                last.then_inc(up_psum, 1)

            up(0)
            up(1)
            pe.wait_ge(share_ready, 1)
            for c in range(NC):
                if c >= 2:
                    pe.wait_ge(shareT_ready, c - 1)
                for t in range(TC):
                    last = nc.tensor.transpose(bank[4 + c % 2][0:E, t * P:(t + 1) * P], share[:, c * TC + t, :], ident[:])
                last.then_inc(shareT_psum, 1)
            for c in range(NC):
                pe.wait_ge(shareT_ready, c + 1)
                if c >= 2:
                    pe.wait_ge(bias3_added, c - 1)
                for t in range(TC):
                    last = nc.tensor.matmul(bank[6 + c % 2][:, t * D:(t + 1) * D], shareT[:, c, t * P:(t + 1) * P], b3[:], start=True, stop=True)
                last.then_inc(bias3_psum, 1)

            pe.wait_ge(shareT_ready, NC)

            def down(k):
                e, c = k // NC, k % NC
                pe.wait_ge(gated_ready, MT * (k + 1))
                if k >= 2:
                    pe.wait_ge(added, k - 1)
                for t in range(TC):
                    for m in range(MT):
                        last = nc.tensor.matmul(bank[4 + k % 2][:, t * D:(t + 1) * D], gated[:, k % 2, m, t * P:(t + 1) * P],
                                                w3[:, e % 2, m, :], start=(m == 0), stop=(m == MT - 1))
                last.then_inc(down_psum, 1)

            for n in range(2, E * NC * MT):
                up(n)
                if n % MT == 1 and n > MT:
                    down(n // MT - 1)
            down(E * NC - 1)


def lay_out(i, np):
    x = i["x"].reshape(T, D)
    context = i["ctx_1024"].reshape(T, D)
    wo = np.zeros((4, 32, GROUPS, D), np.float32)
    wo[:, :HD] = i["L0_xattn_Wo"].reshape(D, GROUPS, 4, HD).transpose(2, 3, 1, 0)
    rows = np.zeros((2, 6, PAIRS * CH), np.uint16)
    rows[0, 0:3] = ONE_BF16
    rows[1, 3:6] = ONE_BF16
    f = {k[len("L0_ffn_"):]: v for k, v in i.items() if k.startswith("L0_ffn_")}
    choice_rows = np.zeros((P, 6), np.float32)
    choice_sel = np.zeros((P, 2, 4, P), np.uint16)
    weight_sel = np.zeros((P, 2, P), np.float32)
    eb2 = np.zeros((P, 3 * D), np.float32)
    for k in range(2):
        for r in range(3):
            choice_rows[32 * k + E * r:32 * k + E * r + E, 3 * k + r] = 1
            eb2[32 * k + E * r:32 * k + E * r + E] = f["expert_b2"]
        for e in range(E):
            choice_sel[32 * k + e, k, e // 2, HID * (e % 2):HID * (e % 2) + HID] = ONE_BF16
        weight_sel[64 + 32 * k, k] = 1
    sw1 = np.zeros((P, 2, 96), np.float32)
    sw1[:, :, :HID] = f["shared_w1"].reshape(2, P, HID).transpose(1, 0, 2)
    sw1[:, 0, HID:] = f["halt_w1"]
    sw2 = np.zeros((96, 3 * D), np.float32)
    sw2[:HID] = f["shared_w2"]
    hw2 = np.zeros((96, P), np.float32)
    hw2[HID:] = f["halt_w2"]
    return {
        "rw1": f["router_w1"], "rw2": f["router_w2"], "rb1": f["router_b1"][:, None], "rb2": f["router_b2"],
        "ew1": f["expert_w1"].transpose(1, 0, 2).reshape(2, P, E * HID).transpose(1, 0, 2),
        "eb1": f["expert_b1"].reshape(4, P).T, "ew2": f["expert_w2"].reshape(4, P, 3 * D).transpose(1, 0, 2),
        "eb2": eb2, "choice_rows": choice_rows, "choice_sel": choice_sel, "weight_sel": weight_sel,
        "sw1": sw1, "sb1": np.concatenate([f["shared_b1"], f["halt_b1"]])[:, None], "sw2": sw2,
        "sb2": f["shared_b2"].reshape(3, P).T, "hw2": hw2, "hb2": f["halt_b2"], "mu": f["mu"][:, None],
        "shared_w": f["shared_weight"].reshape(1), "iota24": np.broadcast_to(np.tile(np.arange(E, dtype=np.float32), 3), (P, 24)),
        "fw1": f["refine_w1"], "fb1": f["refine_b1"].reshape(2, P).T, "fw2": f["refine_w2"].reshape(2, P, D).transpose(1, 0, 2),
        "w1": i["L1_ffn_W1"], "w2": i["L1_ffn_W2"], "w3": i["L1_ffn_W3"].reshape(E, MT, P, D).transpose(0, 2, 1, 3),
        "b12": np.stack([i["L1_ffn_b1"], i["L1_ffn_b2"]]).reshape(2, E, MT, P).transpose(3, 0, 1, 2),
        "b3": i["L1_ffn_b3"], "wr": i["L1_ffn_Wr"], "br": i["L1_ffn_br"],
        "iota8": np.broadcast_to(np.arange(E, dtype=np.float32), (P, E)),
        "iw": f["integration_weight"], "fb2": f["refine_b2"],
        "x": x, "ctx": context, "ctxT": context.T, "ident": np.eye(P, dtype=np.float32),
        "wqT": i["L0_xattn_Wq"].T, "wkT": i["L0_xattn_Wk"].T, "wvT": i["L0_xattn_Wv"].T,
        "wo": wo.reshape(P, GROUPS, D), "max_rows": rows,
        "qk_bias": np.stack([i["L0_xattn_bq"], i["L0_xattn_bk"]], 1),
        "bv": i["L0_xattn_bv"], "bo": i["L0_xattn_bo"],
        "gates": np.broadcast_to(np.concatenate([i["g_xattn"], i["g_ffn"]]), (P, 4)),
    }


_OUTS = [((8, 256, 128), 'float32')]


def kernel(**inputs):
    import numpy as _np
    import concourse.bacc as _bacc
    from concourse import mybir as _mybir
    from concourse.bass_utils import run_bass_kernel_spmd as _run

    c = _np.ascontiguousarray
    i = {k: _np.asarray(v) for k, v in inputs.items()}
    arrays = lay_out(i, _np)
    nc = _bacc.Bacc("TRN2", target_bir_lowering=False, num_devices=1)
    a = {}
    feed = {}
    for name, v in arrays.items():
        v = c(v)
        feed[f"in_{name}_dram"] = v
        a[name] = nc.dram_tensor(f"in_{name}_dram", v.shape, _mybir.dt.from_np(v.dtype), kind="ExternalInput").ap()
    out = nc.dram_tensor("out_0_dram", (T, D), F32, kind="ExternalOutput").ap()
    flamingo(nc, a, out)
    r = _run(nc, [feed], core_ids=[0])
    return r.results[0]["out_0_dram"].reshape(B, S, D)
```
